# Optimizing a Trainium2 kernel written in Bass

```python
import numpy as np
import jax
import jax.numpy as jnp

def _softmax(x, axis=-1):
    return jax.nn.softmax(x, axis=axis)

def _gelu(x):
    return jax.nn.gelu(x, approximate=True)

def _silu(x):
    return jax.nn.silu(x)

def _sigmoid(x):
    return jax.nn.sigmoid(x)

def _layernorm(x, axis=-1, eps=1e-05):
    m = jnp.mean(x, axis=axis, keepdims=True)
    v = jnp.var(x, axis=axis, keepdims=True)
    return (x - m) / jnp.sqrt(v + eps)

def _scatter_add(tgt, idx, src, axis=0):
    return tgt.at[idx].add(src)

def _segment_sum(src, seg, n):
    return jax.ops.segment_sum(src, seg, n)
kernel_name = 'mk_rec_standalone_d1_rec_r8_c6b446'

def setup_inputs(seed: int=0):
    np.random.seed(seed)
    _w = jnp.asarray

    def _rec_inputs():
        import jax
        import jax.numpy as jnp
        _rk = jax.random.key(seed)
        r_decade_idxs = jax.random.randint(jax.random.fold_in(_rk, 1), (1024, 12), 0, 2, jnp.int32)
        r_movie_idxs = jax.random.randint(jax.random.fold_in(_rk, 2), (1024, 7500), 0, 2, jnp.int32)
        r_category_idxs = jax.random.randint(jax.random.fold_in(_rk, 3), (1024, 32), 0, 2, jnp.int32)
        r_person_idxs = jax.random.randint(jax.random.fold_in(_rk, 4), (1024, 12500), 0, 2, jnp.int32)
        r_company_idxs = jax.random.randint(jax.random.fold_in(_rk, 5), (1024, 2500), 0, 2, jnp.int32)
        return (r_decade_idxs, r_movie_idxs, r_category_idxs, r_person_idxs, r_company_idxs)
    r_decade_idxs, r_movie_idxs, r_category_idxs, r_person_idxs, r_company_idxs = _rec_inputs()

    def _L0_rec_setup():
        import jax, jax.numpy as jnp
        import numpy as np
        B = 256
        LF = 64
        N_DEC, N_MOV, N_CAT, N_PER, N_COM = (12, 7500, 32, 12500, 2500)

        def _norm_rows(emb, s):
            mask = s != 0
            safe = jnp.where(mask, s, jnp.ones_like(s))
            return jnp.where(mask[:, None], emb / safe[:, None], emb)
        key = jax.random.key(seed)
        ks = jax.random.split(key, 10)

        def multihot(k, n):
            return jax.random.randint(k, (B, n), 0, 2, dtype=jnp.int32)

        def weight(k, n):
            return jax.random.normal(k, (n, LF), dtype=jnp.float32) * 0.02
        return {'decade_idxs': multihot(ks[0], N_DEC), 'movie_idxs': multihot(ks[1], N_MOV), 'category_idxs': multihot(ks[2], N_CAT), 'person_idxs': multihot(ks[3], N_PER), 'company_idxs': multihot(ks[4], N_COM), 'W_dec': weight(ks[5], N_DEC), 'W_mov': weight(ks[6], N_MOV), 'W_cat': weight(ks[7], N_CAT), 'W_per': weight(ks[8], N_PER), 'W_com': weight(ks[9], N_COM)}
    _L0_rec_all = _L0_rec_setup()
    _L0_rec_in = {k: v for k, v in _L0_rec_all.items() if k in ('W_dec', 'W_mov', 'W_cat', 'W_per', 'W_com')}
    del _L0_rec_all
    return {'r_decade_idxs': r_decade_idxs, 'r_movie_idxs': r_movie_idxs, 'r_category_idxs': r_category_idxs, 'r_person_idxs': r_person_idxs, 'r_company_idxs': r_company_idxs, 'L0_rec_W_dec': _L0_rec_in['W_dec'], 'L0_rec_W_mov': _L0_rec_in['W_mov'], 'L0_rec_W_cat': _L0_rec_in['W_cat'], 'L0_rec_W_per': _L0_rec_in['W_per'], 'L0_rec_W_com': _L0_rec_in['W_com']}

def reference(r_decade_idxs, r_movie_idxs, r_category_idxs, r_person_idxs, r_company_idxs, L0_rec_W_dec, L0_rec_W_mov, L0_rec_W_cat, L0_rec_W_per, L0_rec_W_com):
    import jax
    import jax.numpy as jnp

    def _L0_rec_ref(decade_idxs, movie_idxs, category_idxs, person_idxs, company_idxs, W_dec, W_mov, W_cat, W_per, W_com):
        import jax, jax.numpy as jnp
        import numpy as np
        B = 256
        LF = 64
        N_DEC, N_MOV, N_CAT, N_PER, N_COM = (12, 7500, 32, 12500, 2500)

        def _norm_rows(emb, s):
            mask = s != 0
            safe = jnp.where(mask, s, jnp.ones_like(s))
            return jnp.where(mask[:, None], emb / safe[:, None], emb)
        d = decade_idxs.astype(jnp.float32)
        m = movie_idxs.astype(jnp.float32)
        c = category_idxs.astype(jnp.float32)
        p = person_idxs.astype(jnp.float32)
        q = company_idxs.astype(jnp.float32)
        decades = d @ W_dec
        decades = _norm_rows(decades, jnp.sum(d, axis=1))
        movies = m @ W_mov
        decades = _norm_rows(decades, jnp.sum(m, axis=1))
        categories = _norm_rows(c @ W_cat, jnp.sum(c, axis=1))
        persons = _norm_rows(p @ W_per, jnp.sum(p, axis=1))
        companies = _norm_rows(q @ W_com, jnp.sum(q, axis=1))
        return jnp.concatenate([decades, movies, categories, persons, companies], axis=1)
    y = _L0_rec_ref(r_decade_idxs, r_movie_idxs, r_category_idxs, r_person_idxs, r_company_idxs, L0_rec_W_dec, L0_rec_W_mov, L0_rec_W_cat, L0_rec_W_per, L0_rec_W_com)
    return y

_drawn_inputs = setup_inputs


def setup_inputs(seed=0):
    import zlib

    import numpy as np

    out = dict(_drawn_inputs(seed))
    spreads = {}
    factors = {'L0_rec_W_dec': 200.0, 'L0_rec_W_cat': 8.0, 'L0_rec_W_per': 200.0, 'L0_rec_W_com': 64.0}
    for name, (base, spread) in spreads.items():
        noise = np.random.default_rng([zlib.crc32(name.encode()), seed]).standard_normal(out[name].shape)
        drawn = base * np.exp(spread * noise) if base else spread * noise
        out[name] = jnp.asarray(drawn.astype(out[name].dtype))
    for name, factor in factors.items():
        out[name] = (out[name] * factor).astype(out[name].dtype)
    return out
```

```python
import concourse.bass as bass
from concourse import mybir
from contextlib import ExitStack


def recommender_program(nc, x_dec, x_mov, x_cat, x_per, x_com, w_dec, w_mov, w_cat, w_per, w_com, out):
    fp32, bf16, i32, u32 = mybir.dt.float32, mybir.dt.bfloat16, mybir.dt.int32, mybir.dt.uint32
    ALU = mybir.AluOpType
    AX = mybir.AxisListType
    P = 128

    BATCH = x_mov.shape[0]
    LF = w_mov.shape[1]
    NB = BATCH // P
    NPAIR = NB // 2
    K = 125
    T = 10
    CH = K * T
    WC = 3 * LF + 1
    BANK = 512
    N_DEC, N_CAT = x_dec.shape[1], x_cat.shape[1]
    N_SMALL = N_DEC + N_CAT
    SEGS = []
    first = 0
    for x, w, col in ((x_mov, w_mov, 1), (x_per, w_per, 3), (x_com, w_com, 4)):
        n = x.shape[1] // CH
        SEGS.append((x, w, first, n, col * LF))
        first += n
    CHUNKS = first
    STEPS = CHUNKS * NB
    AHEAD = 2
    P16 = K // 16 * 16

    ctx = ExitStack()
    with ctx:
        def sb(name, shape, dt):
            return ctx.enter_context(nc.sbuf_tensor(name, shape, dt))

        def sem(name):
            return ctx.enter_context(nc.semaphore(name))

        x_int = sb("x_int", [P, NB, CH], i32)
        x_bf = sb("x_bf", [P, 2, T, P], bf16)
        xT = sb("xT", [P, 2, T * P], bf16)
        w_raw = sb("w_raw", [P, 2, T, LF], fp32)
        w_res = sb("w_res", [P, 2, T, LF], fp32)
        w_parts = sb("w_parts", [P, 2, T, WC], bf16)
        sums_sb = sb("sums_sb", [P, len(SEGS), NB, WC], fp32)
        out_sb = sb("out_sb", [P, NB, 5 * LF], fp32)
        dec_once = sb("dec_once", [P, NB, LF], fp32)
        seen = sb("seen", [P, T, P], bf16)
        seen_max = sb("seen_max", [P, 1], fp32)
        bad_f = sb("bad_f", [P, 1], fp32)
        general = sb("general", [1, 1], i32)
        ones_col = sb("ones_col", [P, 1], fp32)
        ident_f = sb("ident_f", [P, P], fp32)
        ident = sb("ident", [P, P], bf16)
        zeros = sb("zeros", [P, BANK], bf16)
        s_int = sb("s_int", [P, NB, N_SMALL], i32)
        s_f = sb("s_f", [P, NB, N_SMALL], fp32)
        s_T = sb("s_T", [N_SMALL, NB * P], fp32)
        s_w = sb("s_w", [N_SMALL, 2 * LF], fp32)
        s_sb = sb("s_sb", [P, NB, 2 * LF], fp32)
        half = sb("half", [P, NB, LF], fp32)
        count = sb("count", [P, 4, NB], fp32)
        safe = sb("safe", [P, 4, NB], fp32)
        recip = sb("recip", [P, 4, NB], fp32)
        recip_mov = sb("recip_mov", [P, NB], fp32)
        g_int = sb("g_int", [P, CH], i32)
        g_f = sb("g_f", [P, T, K], fp32)
        g_T = sb("g_T", [K, T * P], fp32)
        g_w = sb("g_w", [K, T, LF + 1], fp32)
        g_sb = sb("g_sb", [P, LF + 1], fp32)
        g_out = sb("g_out", [P, LF], fp32)
        g_dec = sb("g_dec", [P, LF], fp32)
        g_small = sb("g_small", [P, 4], fp32)

        acc = ctx.enter_context(nc.psum_tensor("acc", [P, NPAIR * BANK], fp32))
        tp = ctx.enter_context(nc.psum_tensor("tp", [P, 2, 4 * BANK], bf16))
        tp_f = tp[:, :, :].rearrange("p a n -> p (a n)").bitcast(fp32)

        x_loaded = [sem(f"x_loaded{b}") for b in range(NB)]
        w_loaded = [sem(f"w_loaded{h}") for h in range(2)]
        small_loaded = sem("small_loaded")
        ident_ready = sem("ident_ready")
        filled = sem("filled")
        s_w_clear = sem("s_w_clear")
        zeroed = sem("zeroed")
        w_step = sem("w_step")
        w_split = sem("w_split")
        maxed = sem("maxed")
        cast = sem("cast")
        transposed = sem("transposed")
        evacuated = sem("evacuated")
        multiplied = sem("multiplied")
        saved = sem("saved")
        small_cast = sem("small_cast")
        small_tp = sem("small_tp")
        small_T = sem("small_T")
        small_done = sem("small_done")
        dve_step = sem("dve_step")
        bad_ready = sem("bad_ready")
        bad_summed = sem("bad_summed")
        general_ready = sem("general_ready")
        finished = sem("finished")
        stored = sem("stored")
        sp_holds, pool_holds, pe_holds = sem("sp_holds"), sem("pool_holds"), sem("pe_holds")
        g_x_loaded = sem("g_x_loaded")
        g_w_loaded = sem("g_w_loaded")
        g_cast = sem("g_cast")
        g_tp = sem("g_tp")
        g_xT = sem("g_xT")
        g_mult = sem("g_mult")
        g_saved = sem("g_saved")
        g_step = sem("g_step")
        g_fin = sem("g_fin")
        g_stored = sem("g_stored")

        def acc_at(pair, h, n):
            return acc[:, bass.ds(pair * BANK + h * WC, n)]

        def x_slice(x, b, chunk):
            return x[b * P:(b + 1) * P, bass.ds(chunk * CH, CH)]

        def w_slice(w, chunk, lo, hi):
            rows = w[bass.ds(chunk * CH + lo * T, (hi - lo) * T), :]
            return rows.rearrange("(p t) f -> p t f", t=T)

        out_t = out.rearrange("(b p) c -> p b c", p=P)
        N_SMALL_LOADS = 4
        N_STORES = 2 + NPAIR

        def hold(eng, semaphore, value, own):
            eng.wait_ge(semaphore, value)
            eng.sem_inc(own, 1)

        block = ctx.enter_context(nc.Block())

        @block.sync
        def _(sp):
            def load_x(seg, c, local, b, wait):
                if wait:
                    hold(sp, cast, c * NB + (b - NB + 1), sp_holds)
                sp.dma_start(x_int[:, b, :], x_slice(SEGS[seg][0], b, local)).then_inc(x_loaded[b], 16)

            def load_w(seg, c, local, h, wait):
                if wait:
                    sp.wait_ge(w_split, c - 1)
                w = SEGS[seg][1]
                for lo, hi in ((0, P16), (P16, K)):
                    sp.dma_start(w_raw[lo:hi, h], w_slice(w, local, lo, hi)).then_inc(w_loaded[h], 16)

            def load_pair(seg, local, base, first, next_seg):
                c = base + local
                for b in range(NB):
                    load_x(seg, c, local, b, not first)
                    if b == 0:
                        load_w(seg, c + 1, local + 1, 1, not first)
                for b in range(NB):
                    load_x(seg, c + 1, local + 1, b, True)
                    if b == 0 and next_seg == seg:
                        load_w(seg, c + 2, local + 2, 0, True)
                    elif b == 0 and next_seg is not None:
                        load_w(next_seg, c + 2, 0, 0, True)

            load_w(0, 0, 0, 0, False)
            for s, (_, _, base, n, _) in enumerate(SEGS):
                last = n - 2
                begin = 0
                if s == 0:
                    load_pair(s, 0, base, True, s)
                    begin = 2
                if last > begin:
                    with sp.Fori(begin, last, 2) as local:
                        load_pair(s, local, base, False, s)
                load_pair(s, last, base, False, s + 1 if s + 1 < len(SEGS) else None)

            sp.wait_ge(finished, 1)
            sp.dma_start(out_t[:, :, 0:3 * LF], out_sb[:, :, 0:3 * LF]).then_inc(stored, 16)
            sp.wait_ge(finished, 2)
            sp.dma_start(out_t[:, :, 3 * LF:4 * LF], out_sb[:, :, 3 * LF:4 * LF]).then_inc(stored, 16)
            for p in range(NPAIR):
                sp.wait_ge(finished, 3 + p)
                sp.dma_start(out_t[:, 2 * p:2 * p + 2, 4 * LF:],
                             out_sb[:, 2 * p:2 * p + 2, 4 * LF:]).then_inc(stored, 16)
            sp.wait_ge(filled, 3)
            sp.wait_ge(general_ready, 1)
            sp.wait_ge(stored, 16 * N_STORES)
            with sp.If(sp.value_load(general[0:1, 0:1], min_val=0, max_val=P) > 0):
                k0 = 0
                for s, (x, w, _, n, col) in enumerate(SEGS):
                    with sp.Fori(0, NB) as b:
                        with sp.Fori(0, n) as c:
                            sp.wait_ge(g_mult, b * n + c + (k0 + 1))
                            sp.dma_start(g_int[:, :], x[bass.ds(b * P, P), bass.ds(c * CH, CH)]).then_inc(g_x_loaded, 16)
                            for lo, hi in ((0, P16), (P16, K)):
                                sp.dma_start(g_w[lo:hi, :, 0:LF], w_slice(w, c, lo, hi)).then_inc(g_w_loaded, 16)
                        sp.wait_ge(g_fin, b + (s * NB + 2))
                        sp.dma_start(out[bass.ds(b * P, P), col:col + LF], g_out[:, :]).then_inc(g_stored, 16)
                        dst = out[bass.ds(b * P, P), 0:LF] if s == 0 else out[bass.ds(b * P, P), col:col + LF]
                        if s == 0:
                            sp.dma_start(dst, g_dec[:, :]).then_inc(g_stored, 16)
                        else:
                            sp.sem_inc(g_stored, 16)
                    k0 += NB * n
                sp.wait_ge(g_stored, 32 * (len(SEGS) * NB + 1))

        @block.gpsimd
        def _(pool):
            chain = [0]

            def link(ins):
                chain[0] += 1
                ins.then_inc(w_step, 1)
                pool.wait_ge(w_step, chain[0])

            link(nc.gpsimd.memset(ident_f[:], 0.0))
            nc.gpsimd.affine_select(out=ident_f[:], in_=ident_f[:], compare_op=ALU.not_equal, fill=1.0, base=0,
                                    pattern=[[-1, P]], channel_multiplier=1).then_inc(ident_ready, 1)
            pool.wait_ge(ident_ready, 1)
            nc.gpsimd.tensor_copy(ident[:], ident_f[:]).then_inc(ident_ready, 1)
            nc.gpsimd.memset(w_parts[:, :, :, 3 * LF:], 1.0).then_inc(filled, 1)
            nc.gpsimd.memset(ones_col[:], 1.0).then_inc(filled, 1)
            pool.wait_ge(w_split, 1)
            base_step = chain[0]

            def split(c, use, h, wait):
                pool.wait_ge(w_loaded[h], use * 32 + 32)
                if wait:
                    hold(pool, multiplied, c * NB + (AHEAD - NB), pool_holds)
                high = w_parts[0:K, h, :, 0:LF]
                middle = w_parts[0:K, h, :, LF:2 * LF]
                low = w_parts[0:K, h, :, 2 * LF:3 * LF]
                raw, rest = w_raw[0:K, h], w_res[0:K, h]
                nc.gpsimd.tensor_copy(high, raw).then_inc(w_step, 1)
                pool.wait_ge(w_step, c * 4 + (base_step - 3))
                nc.gpsimd.tensor_tensor(out=rest, in0=raw, in1=high, op=ALU.subtract).then_inc(w_step, 1)
                hold(pool, w_step, c * 4 + (base_step - 2), pool_holds)
                nc.gpsimd.tensor_copy(middle, rest).then_inc(w_step, 1)
                pool.wait_ge(w_step, c * 4 + (base_step - 1))
                nc.gpsimd.tensor_tensor(out=rest, in0=rest, in1=middle, op=ALU.subtract).then_inc(w_step, 1)
                hold(pool, w_step, c * 4 + (base_step - 0), pool_holds)
                nc.gpsimd.tensor_copy(low, rest).then_inc(w_split, 1)

            split(1, 0, 1, False)
            nc.gpsimd.memset(g_w[:], 1.0).then_inc(filled, 1)
            with pool.Fori(1, CHUNKS // 2) as i:
                for h in range(2):
                    split(i * 2 + h, i, h, True)

        @block.scalar
        def _(act):
            act.dma_start(s_int[:, :, 0:N_DEC], x_dec.rearrange("(b p) n -> p b n", p=P)).then_inc(small_loaded, 16)
            act.dma_start(s_int[:, :, N_DEC:], x_cat.rearrange("(b p) n -> p b n", p=P)).then_inc(small_loaded, 16)
            act.wait_ge(s_w_clear, 1)
            act.dma_start(s_w[0:N_DEC, 0:LF], w_dec).then_inc(small_loaded, 16)
            act.dma_start(s_w[N_DEC:, LF:], w_cat).then_inc(small_loaded, 16)
            act.sem_inc(evacuated, 1)
            act.wait_ge(small_tp, 1)
            nc.scalar.copy(s_T[:, :], tp_f[0:N_SMALL, 0:NB * P]).then_inc(small_T, 1)
            for p in range(NPAIR):
                act.wait_ge(small_done, p + 1)
                nc.scalar.copy(s_sb[:, 2 * p:2 * p + 2, :],
                               acc[:, p * BANK:p * BANK + 2 * WC].rearrange("p (h n) -> p h n", h=2)[:, :, 0:2 * LF]
                               ).then_inc(saved, 1)

            def evacuate(s, h):
                act.wait_ge(transposed, s + (1 + AHEAD))
                act.wait_ge(multiplied, s + 1)
                nc.scalar.copy(xT[:, h, :], tp[:, h, 0:T * P]).then_inc(evacuated, 1)

            def save(seg, s_last, p):
                act.wait_ge(multiplied, s_last + (1 + AHEAD))
                nc.scalar.copy(sums_sb[:, seg, 2 * p:2 * p + 2, :],
                               acc[:, p * BANK:p * BANK + 2 * WC].rearrange("p (h n) -> p h n", h=2)
                               ).then_inc(saved, 1)

            for seg, (_, _, base, n, _) in enumerate(SEGS):
                with act.Fori(base * NPAIR, (base + n - 1) * NPAIR) as q:
                    for h in range(2):
                        evacuate(q * 2 + h, h)
                s0 = (base + n - 1) * NB
                for p in range(NPAIR):
                    for h in range(2):
                        evacuate(s0 + 2 * p + h, h)
                    if p:
                        save(seg, s0 + 2 * p - 1, p - 1)
                save(seg, s0 + NB - 1, NPAIR - 1)

            act.wait_ge(general_ready, 1)
            with act.If(act.value_load(general[0:1, 0:1], min_val=0, max_val=P) > 0):
                k0 = 0
                for s, (x, w, _, n, col) in enumerate(SEGS):
                    with act.Fori(0, NB) as b:
                        with act.Fori(0, n) as c:
                            act.wait_ge(g_tp, b * n + c + (k0 + 1))
                            nc.scalar.copy(g_T[:, :], tp_f[0:K, 0:T * P]).then_inc(g_xT, 1)
                        act.wait_ge(g_mult, b * n + (k0 + n + 1))
                        act.wait_ge(g_fin, b + (s * NB + 1))
                        nc.scalar.copy(g_sb[:, :], acc[:, 0:LF + 1]).then_inc(g_saved, 1)
                    k0 += NB * n

        @block.vector
        def _(dve):
            chain = [0]

            def link(ins):
                chain[0] += 1
                ins.then_inc(dve_step, 1)
                dve.wait_ge(dve_step, chain[0])

            def reciprocal_counts(slot, lo, hi):
                c, s, r = count[:, slot, lo:hi], safe[:, slot, lo:hi], recip[:, slot, lo:hi]
                link(nc.vector.tensor_scalar(s, c, 0.0, None, ALU.is_equal))
                link(nc.vector.tensor_tensor(s, s, c, ALU.add))
                link(nc.vector.reciprocal(r, s))
                return r

            def across(r, n):
                return r.unsqueeze(2).to_broadcast([P, n, LF])

            def small_finish():
                dve.wait_ge(saved, NPAIR)
                for slot, (a, z) in enumerate(((0, N_DEC), (N_DEC, N_SMALL))):
                    link(nc.vector.tensor_reduce(count[:, slot, :], s_f[:, :, a:z], AX.X, ALU.add))
                    r = reciprocal_counts(slot, 0, NB)
                    dst = dec_once[:, :, :] if slot == 0 else out_sb[:, :, 2 * LF:3 * LF]
                    link(nc.vector.tensor_tensor(dst, s_sb[:, :, slot * LF:(slot + 1) * LF], across(r, NB), ALU.mult))

            def finish(seg, lo, hi):
                sums = sums_sb[:, seg, lo:hi, :]
                n = hi - lo
                col = SEGS[seg][4]
                dst = out_sb[:, lo:hi, col:col + LF]
                dve.wait_ge(saved, NPAIR * (seg + 1) + hi // 2)
                link(nc.vector.tensor_tensor(half[:, lo:hi], sums[:, :, LF:2 * LF], sums[:, :, 2 * LF:3 * LF], ALU.add))
                link(nc.vector.tensor_scalar(count[:, 2, lo:hi], sums[:, :, 3 * LF], 1.0, None, ALU.mult))
                r = reciprocal_counts(2, lo, hi)
                if seg == 0:
                    link(nc.vector.tensor_tensor(dst, half[:, lo:hi], sums[:, :, 0:LF], ALU.add))
                    nc.vector.tensor_tensor(out_sb[:, lo:hi, 0:LF], dec_once[:, lo:hi], across(r, n),
                                            ALU.mult).then_inc(finished, 1)
                else:
                    link(nc.vector.tensor_tensor(half[:, lo:hi], half[:, lo:hi], sums[:, :, 0:LF], ALU.add))
                    nc.vector.tensor_tensor(dst, half[:, lo:hi], across(r, n), ALU.mult).then_inc(finished, 1)

            def round_chunk(c):
                for p in range(NPAIR):
                    for h in range(2):
                        b = 2 * p + h
                        dve.wait_ge(x_loaded[b], c * 16 + 16)
                        dve.wait_ge(transposed, c * NB + (b + 1))
                        nc.vector.tensor_copy(x_bf[:, h, :, 0:K],
                                              x_int[:, b, :].bitcast(u32).rearrange("p (k t) -> p t k", t=T)
                                              ).then_inc(cast, 1)
                        dve.wait_ge(cast, c * NB + (b + 1))
                        if not (isinstance(c, int) and c == 0 and b == 0):
                            dve.wait_ge(maxed, c * NB + b)
                        nc.vector.tensor_tensor(seen[:, :, :], seen[:, :, :], x_bf[:, h, :, :], ALU.max).then_inc(maxed, 1)

            nc.vector.memset(s_w[:], 0.0).then_inc(s_w_clear, 1)
            nc.vector.memset(zeros[:].bitcast(u32), 0).then_inc(zeroed, 1)
            link(nc.vector.memset(x_bf[:, :, :, K:].rearrange("p h t k -> p (h t) k"), 0.0))
            link(nc.vector.memset(w_parts[96:, :, :, 0:3 * LF], 0.0))
            link(nc.vector.memset(seen[:].bitcast(u32), 0))

            dve.wait_ge(w_loaded[0], 32)
            rest, raw = w_res[0:K, 0], w_raw[0:K, 0]
            high, middle, low = (w_parts[0:K, 0, :, n * LF:(n + 1) * LF] for n in range(3))
            link(nc.vector.tensor_copy(high, raw))
            link(nc.vector.tensor_tensor(rest, raw, high, ALU.subtract))
            link(nc.vector.tensor_copy(middle, rest))
            link(nc.vector.tensor_tensor(rest, rest, middle, ALU.subtract))
            nc.vector.tensor_copy(low, rest).then_inc(w_split, 1)

            dve.wait_ge(small_loaded, 64)
            nc.vector.tensor_copy(s_f[:, :, :], s_int[:, :, :]).then_inc(small_cast, 1)
            for seg, (_, _, base, n, _) in enumerate(SEGS):
                round_chunk(base)
                if seg == 0:
                    small_finish()
                else:
                    finish(seg - 1, 0, NB)
                with dve.Fori(base + 1, base + n) as c:
                    round_chunk(c)

            for p in range(NPAIR):
                finish(len(SEGS) - 1, 2 * p, 2 * p + 2)
            dve.wait_ge(maxed, STEPS)
            link(nc.vector.tensor_reduce(seen_max[:], seen[:].rearrange("p t k -> p (t k)"), AX.X, ALU.max))
            nc.vector.tensor_scalar(bad_f[:], seen_max[:], 1.0, None, ALU.is_gt).then_inc(bad_ready, 1)
            dve.wait_ge(bad_summed, 1)
            nc.vector.tensor_copy(general[:], tp_f[0:1, 0:1]).then_inc(general_ready, 1)
            dve.wait_ge(general_ready, 1)
            with dve.If(dve.value_load(general[0:1, 0:1], min_val=0, max_val=P) > 0):
                k0 = 0
                for s, (x, w, _, n, col) in enumerate(SEGS):
                    with dve.Fori(0, NB) as b:
                        with dve.Fori(0, n) as c:
                            dve.wait_ge(g_x_loaded, (b * n + c + (k0 + 1)) * 16)
                            nc.vector.tensor_copy(g_f[:, :, :], g_int[:, :].rearrange("p (k t) -> p t k", t=T)
                                                  ).then_inc(g_cast, 1)
                        dve.wait_ge(g_saved, b + (s * NB + 2))
                        dve.wait_ge(g_stored, b * 32 + (s * NB * 32 + 32))
                        steps = b * 4 + s * NB * 4
                        total = g_sb[:, LF:LF + 1]
                        nc.vector.tensor_scalar(g_small[:, 0:1], total, 0.0, None, ALU.is_equal).then_inc(g_step, 1)
                        dve.wait_ge(g_step, steps + 1)
                        nc.vector.tensor_tensor(g_small[:, 1:2], g_small[:, 0:1], total, ALU.add).then_inc(g_step, 1)
                        dve.wait_ge(g_step, steps + 2)
                        nc.vector.reciprocal(g_small[:, 2:3], g_small[:, 1:2]).then_inc(g_step, 1)
                        dve.wait_ge(g_step, steps + 3)
                        if s == 0:
                            nc.vector.tensor_copy(g_out[:], g_sb[:, 0:LF]).then_inc(g_step, 1)
                            dve.wait_ge(g_step, steps + 4)
                            nc.vector.tensor_scalar(g_dec[:], dec_once[:, bass.ds(b, 1), :].rearrange("p a f -> p (a f)"),
                                                    g_small[:, 2:3], None, ALU.mult).then_inc(g_fin, 1)
                        else:
                            nc.vector.tensor_copy(g_small[:, 3:4], g_small[:, 2:3]).then_inc(g_step, 1)
                            dve.wait_ge(g_step, steps + 4)
                            nc.vector.tensor_scalar(g_out[:], g_sb[:, 0:LF], g_small[:, 3:4], None,
                                                    ALU.mult).then_inc(g_fin, 1)
                    k0 += NB * n

        @block.tensor
        def _(pe):
            pe.wait_ge(ident_ready, 2)
            pe.wait_ge(small_cast, 1)
            for b in range(NB):
                last = nc.tensor.transpose(tp_f[0:N_SMALL, b * P:(b + 1) * P], s_f[:, b, :], ident_f[:, :])
            last.then_inc(small_tp, 1)
            pe.wait_ge(small_T, 1)
            pe.wait_ge(small_loaded, 64)
            for b in range(NB):
                last = nc.tensor.matmul(acc_at(b // 2, b % 2, 2 * LF), s_T[:, b * P:(b + 1) * P], s_w[:, :],
                                        start=True, stop=True)
                if b % 2:
                    last.then_inc(small_done, 1)
            pe.sem_inc(transposed, AHEAD)
            pe.sem_inc(multiplied, AHEAD)

            def transpose_step(s, h):
                pe.wait_ge(cast, s + 1)
                if not isinstance(s, int) or s >= 2:
                    pe.wait_ge(evacuated, s)
                for t in range(T):
                    last = nc.tensor.transpose(tp[:, h, t * P:(t + 1) * P], x_bf[:, h, t, :], ident[:, :])
                last.then_inc(transposed, 1)

            def multiply_step(s, h, wh, pair):
                pe.wait_ge(evacuated, s + 2)
                for t in range(T):
                    last = nc.tensor.matmul(acc_at(pair, h, WC), xT[:, h, t * P:(t + 1) * P], w_parts[:, wh, t, :],
                                            start=False, stop=(t == T - 1), skip_group_check=True)
                last.then_inc(multiplied, 1)

            transpose_step(0, 0)
            pe.wait_ge(filled, 2)
            pe.wait_ge(zeroed, 1)
            for seg, (_, _, base, n, _) in enumerate(SEGS):
                for p in range(NPAIR):
                    pe.wait_ge(saved, seg * NPAIR + p + 1)
                    nc.tensor.matmul(acc[:, p * BANK:(p + 1) * BANK], zeros[:, 0:P], zeros[:, :],
                                     start=True, stop=True)
                final = seg == len(SEGS) - 1
                with ExitStack() as pairs:
                    i = pairs.enter_context(pe.Fori(0, n // 2)) if n > 2 else 0
                    for wh in range(2):
                        c = i * 2 + (base + wh)
                        hold(pe, w_split, c + 1, pe_holds)
                        rolled = NPAIR - 1 if final and wh == 1 else NPAIR
                        with pe.Fori(0, rolled) as pair:
                            for h in range(2):
                                s = c * NB + pair * 2 + h
                                transpose_step(s + 1, 1 - h)
                                multiply_step(s, h, wh, pair)
                        if rolled < NPAIR:
                            transpose_step(STEPS - 1, 1)
                            multiply_step(STEPS - 2, 0, wh, NPAIR - 1)
                            multiply_step(STEPS - 1, 1, wh, NPAIR - 1)

            pe.wait_ge(bad_ready, 1)
            nc.tensor.matmul(tp_f[0:1, 0:1], bad_f[:, :], ones_col[:, :], start=True, stop=True).then_inc(bad_summed, 1)
            pe.wait_ge(general_ready, 1)
            with pe.If(pe.value_load(general[0:1, 0:1], min_val=0, max_val=P) > 0):
                pe.wait_ge(filled, 3)
                pe.sem_inc(g_mult, 1)
                pe.sem_inc(g_stored, 32)
                pe.sem_inc(g_fin, 1)
                pe.sem_inc(g_saved, 1)
                pe.wait_ge(saved, (len(SEGS) + 1) * NPAIR)
                k0 = 0
                for s, (x, w, _, n, col) in enumerate(SEGS):
                    with pe.Fori(0, NB) as b:
                        pe.wait_ge(g_saved, b + (s * NB + 1))
                        nc.tensor.matmul(acc[:, 0:LF + 1], zeros[:, 0:P], zeros[:, 0:LF + 1], start=True, stop=True)
                        with pe.Fori(0, n) as c:
                            k = b * n + c + k0
                            pe.wait_ge(g_cast, k + 1)
                            for t in range(T):
                                last = nc.tensor.transpose(tp_f[0:K, t * P:(t + 1) * P], g_f[:, t, :], ident_f[:, :])
                            last.then_inc(g_tp, 1)
                            pe.wait_ge(g_xT, k + 1)
                            pe.wait_ge(g_w_loaded, (k + 1) * 32)
                            for t in range(T):
                                last = nc.tensor.matmul(acc[:, 0:LF + 1], g_T[:, t * P:(t + 1) * P], g_w[:, t, :],
                                                        start=False, stop=(t == T - 1), skip_group_check=True)
                            last.then_inc(g_mult, 1)
                    k0 += NB * n


_INS = ['r_decade_idxs', 'r_movie_idxs', 'r_category_idxs', 'r_person_idxs', 'r_company_idxs',
        'L0_rec_W_dec', 'L0_rec_W_mov', 'L0_rec_W_cat', 'L0_rec_W_per', 'L0_rec_W_com']


def kernel(**inputs):
    import numpy as _np
    import concourse.bacc as _bacc
    from concourse import mybir as _mybir
    from concourse.bass_utils import run_bass_kernel_spmd as _run

    nc = _bacc.Bacc("TRN2", target_bir_lowering=False, num_devices=1)
    arrays, args = {}, []
    for name in _INS:
        a = _np.ascontiguousarray(inputs[name])
        arrays[f"in_{name}_dram"] = a
        args.append(nc.dram_tensor(f"in_{name}_dram", a.shape, _mybir.dt.from_np(a.dtype), kind="ExternalInput").ap())
    rows = inputs['r_movie_idxs'].shape[0]
    cols = 5 * inputs['L0_rec_W_mov'].shape[1]
    out = nc.dram_tensor("out_0_dram", (rows, cols), _mybir.dt.float32, kind="ExternalOutput").ap()
    recommender_program(nc, *args, out)
    r = _run(nc, [arrays], core_ids=[0])
    return r.results[0]["out_0_dram"]
```

```python
import concourse.bass as bass
from concourse import mybir
from contextlib import ExitStack


def recommender_program(nc, x_dec, x_mov, x_cat, x_per, x_com, w_dec, w_mov, w_cat, w_per, w_com, out):
    fp32, bf16, i32, u32 = mybir.dt.float32, mybir.dt.bfloat16, mybir.dt.int32, mybir.dt.uint32
    ALU = mybir.AluOpType
    ACT = mybir.ActivationFunctionType
    AX = mybir.AxisListType
    P = 128

    BATCH = x_mov.shape[0]
    LF = w_mov.shape[1]
    NB = BATCH // P
    NPAIR = NB // 2
    K = 125
    T = 10
    CH = K * T
    WC = 3 * LF + 1
    BANK = 512
    N_DEC, N_CAT = x_dec.shape[1], x_cat.shape[1]
    N_SMALL = N_DEC + N_CAT
    SEGS = []
    first = 0
    for x, w, col in ((x_mov, w_mov, 1), (x_per, w_per, 3), (x_com, w_com, 4)):
        n = x.shape[1] // CH
        SEGS.append((x, w, first, n, col * LF))
        first += n
    CHUNKS = first
    STEPS = CHUNKS * NB
    LAST = len(SEGS) - 1
    AHEAD = 2
    P16 = K // 16 * 16

    ctx = ExitStack()
    with ctx:
        def sb(name, shape, dt):
            return ctx.enter_context(nc.sbuf_tensor(name, shape, dt))

        def sem(name):
            return ctx.enter_context(nc.semaphore(name))

        x_int = sb("x_int", [P, NB, CH], i32)
        x_bf = sb("x_bf", [P, 2, T, P], bf16)
        xT = sb("xT", [P, 2, T * P], bf16)
        w_raw = sb("w_raw", [P, 2, T, LF], fp32)
        w_res = sb("w_res", [P, 2, T, LF], fp32)
        w_parts = sb("w_parts", [P, 2, T, WC], bf16)
        sums_sb = sb("sums_sb", [P, len(SEGS), NB, WC], fp32)
        out_sb = sb("out_sb", [P, NB, 5 * LF], fp32)
        dec_once = sb("dec_once", [P, NB, LF], fp32)
        seen = sb("seen", [P, T, P], bf16)
        minus_one = sb("minus_one", [P, 1], fp32)
        excess = sb("excess", [P, T * P], bf16)
        bad_f = sb("bad_f", [P, 1], fp32)
        general = sb("general", [1, 1], i32)
        ones_col = sb("ones_col", [P, 1], fp32)
        ident_f = sb("ident_f", [P, P], fp32)
        ident = sb("ident", [P, P], bf16)
        zeros = sb("zeros", [P, BANK], bf16)
        s_int = sb("s_int", [P, NB, N_SMALL], i32)
        s_f = sb("s_f", [P, NB, N_SMALL], fp32)
        s_T = sb("s_T", [N_SMALL, NB * P], fp32)
        s_w = sb("s_w", [N_SMALL, 2 * LF], fp32)
        s_sb = sb("s_sb", [P, NB, 2 * LF], fp32)
        half = sb("half", [P, NB, LF], fp32)
        whole = sb("whole", [P, NB, LF], fp32)
        count = sb("count", [P, 2, NB], fp32)
        safe = sb("safe", [P, 3, NB], fp32)
        recip = sb("recip", [P, 3, NB], fp32)
        g_int = sb("g_int", [P, CH], i32)
        g_f = sb("g_f", [P, T, K], fp32)
        g_T = sb("g_T", [K, T * P], fp32)
        g_w = sb("g_w", [K, T, LF + 1], fp32)
        g_sb = sb("g_sb", [P, LF + 1], fp32)
        g_out = sb("g_out", [P, LF], fp32)
        g_dec = sb("g_dec", [P, LF], fp32)
        g_zero = sb("g_zero", [P, 1], fp32)
        g_safe = sb("g_safe", [P, 1], fp32)
        g_recip = sb("g_recip", [P, 1], fp32)

        acc = ctx.enter_context(nc.psum_tensor("acc", [P, NPAIR * BANK], fp32))
        tp = ctx.enter_context(nc.psum_tensor("tp", [P, 2, 4 * BANK], bf16))
        tp_f = tp[:, :, :].rearrange("p a n -> p (a n)").bitcast(fp32)

        x_loaded = [sem(f"x_loaded{b}") for b in range(NB)]
        w_loaded = [sem(f"w_loaded{h}") for h in range(2)]
        small_loaded = sem("small_loaded")
        ident_ready = sem("ident_ready")
        filled = sem("filled")
        s_w_clear = sem("s_w_clear")
        zeroed = sem("zeroed")
        w_step = sem("w_step")
        w_split = sem("w_split")
        maxed = sem("maxed")
        cast = sem("cast")
        transposed = sem("transposed")
        evacuated = sem("evacuated")
        multiplied = sem("multiplied")
        saved = sem("saved")
        small_cast = sem("small_cast")
        small_tp = sem("small_tp")
        small_T = sem("small_T")
        small_done = sem("small_done")
        dve_step = sem("dve_step")
        minus_one_ready = sem("minus_one_ready")
        bad_ready = sem("bad_ready")
        bad_summed = sem("bad_summed")
        general_ready = sem("general_ready")
        finished = sem("finished")
        stored = sem("stored")
        sp_holds, pool_holds, pe_holds = sem("sp_holds"), sem("pool_holds"), sem("pe_holds")
        g_x_loaded = sem("g_x_loaded")
        g_w_loaded = sem("g_w_loaded")
        g_cast = sem("g_cast")
        g_tp = sem("g_tp")
        g_xT = sem("g_xT")
        g_mult = sem("g_mult")
        g_saved = sem("g_saved")
        g_step = sem("g_step")
        g_fin = sem("g_fin")
        g_stored = sem("g_stored")

        def acc_at(pair, h, n):
            return acc[:, bass.ds(pair * BANK + h * WC, n)]

        def x_slice(x, b, chunk):
            return x[b * P:(b + 1) * P, bass.ds(chunk * CH, CH)]

        def w_slice(w, chunk, lo, hi):
            rows = w[bass.ds(chunk * CH + lo * T, (hi - lo) * T), :]
            return rows.rearrange("(p t) f -> p t f", t=T)

        out_t = out.rearrange("(b p) c -> p b c", p=P)
        N_SMALL_LOADS = 4
        N_STORES = 2 + NPAIR

        G_STORES = (2, 1, 1)
        G_STEPS = (4, 3, 3)

        def hold(eng, semaphore, value, own):
            eng.wait_ge(semaphore, value)
            eng.sem_inc(own, 1)

        block = ctx.enter_context(nc.Block())

        @block.sync
        def _(sp):
            def load_x(seg, c, local, b, wait):
                if wait:
                    hold(sp, cast, c * NB + (b - NB + 1), sp_holds)
                sp.dma_start(x_int[:, b, :], x_slice(SEGS[seg][0], b, local)).then_inc(x_loaded[b], 16)

            def load_w(seg, c, local, h, wait):
                if wait:
                    sp.wait_ge(w_split, c - 1)
                w = SEGS[seg][1]
                for lo, hi in ((0, P16), (P16, K)):
                    sp.dma_start(w_raw[lo:hi, h], w_slice(w, local, lo, hi)).then_inc(w_loaded[h], 16)

            def load_pair(seg, local, base, first, next_seg):
                c = base + local
                for b in range(NB):
                    load_x(seg, c, local, b, not first)
                    if b == 0:
                        load_w(seg, c + 1, local + 1, 1, not first)
                for b in range(NB):
                    load_x(seg, c + 1, local + 1, b, True)
                    if b == 0 and next_seg == seg:
                        load_w(seg, c + 2, local + 2, 0, True)
                    elif b == 0 and next_seg is not None:
                        load_w(next_seg, c + 2, 0, 0, True)

            load_w(0, 0, 0, 0, False)
            for s, (_, _, base, n, _) in enumerate(SEGS):
                last = n - 2
                begin = 0
                if s == 0:
                    load_pair(s, 0, base, True, s)
                    begin = 2
                if last > begin:
                    with sp.Fori(begin, last, 2) as local:
                        load_pair(s, local, base, False, s)
                load_pair(s, last, base, False, s + 1 if s + 1 < len(SEGS) else None)

            sp.wait_ge(finished, 1)
            sp.dma_start(out_t[:, :, 0:3 * LF], out_sb[:, :, 0:3 * LF]).then_inc(stored, 16)
            sp.wait_ge(finished, 2)
            sp.dma_start(out_t[:, :, 3 * LF:4 * LF], out_sb[:, :, 3 * LF:4 * LF]).then_inc(stored, 16)
            for p in range(NPAIR):
                sp.wait_ge(finished, 3 + p)
                sp.dma_start(out_t[:, 2 * p:2 * p + 2, 4 * LF:],
                             out_sb[:, 2 * p:2 * p + 2, 4 * LF:]).then_inc(stored, 16)
            sp.wait_ge(filled, 3)
            sp.wait_ge(general_ready, 1)
            sp.wait_ge(stored, 16 * N_STORES)
            with sp.If(sp.value_load(general[0:1, 0:1], min_val=0, max_val=1) > 0):
                k0 = 0
                for s, (x, w, _, n, col) in enumerate(SEGS):
                    with sp.Fori(0, NB) as b:
                        with sp.Fori(0, n) as c:
                            sp.wait_ge(g_mult, b * n + c + (k0 + 1))
                            sp.dma_start(g_int[:, :], x[bass.ds(b * P, P), bass.ds(c * CH, CH)]).then_inc(g_x_loaded, 16)
                            for lo, hi in ((0, P16), (P16, K)):
                                sp.dma_start(g_w[lo:hi, :, 0:LF], w_slice(w, c, lo, hi)).then_inc(g_w_loaded, 16)
                        sp.wait_ge(g_fin, b + (s * NB + 2))
                        sp.dma_start(out[bass.ds(b * P, P), col:col + LF], g_out[:, :]).then_inc(g_stored, 16)
                        if s == 0:
                            sp.dma_start(out[bass.ds(b * P, P), 0:LF], g_dec[:, :]).then_inc(g_stored, 16)
                    k0 += NB * n
                sp.wait_ge(g_stored, 16 + sum(16 * NB * stores for stores in G_STORES))

        @block.gpsimd
        def _(pool):
            chain = [0]

            def link(ins):
                chain[0] += 1
                ins.then_inc(w_step, 1)
                pool.wait_ge(w_step, chain[0])

            link(nc.gpsimd.memset(ident_f[:], 0.0))
            nc.gpsimd.affine_select(out=ident_f[:], in_=ident_f[:], compare_op=ALU.not_equal, fill=1.0, base=0,
                                    pattern=[[-1, P]], channel_multiplier=1).then_inc(ident_ready, 1)
            pool.wait_ge(ident_ready, 1)
            nc.gpsimd.tensor_copy(ident[:], ident_f[:]).then_inc(ident_ready, 1)
            nc.gpsimd.memset(w_parts[:, :, :, 3 * LF:], 1.0).then_inc(filled, 1)
            nc.gpsimd.memset(ones_col[:], 1.0).then_inc(filled, 1)
            pool.wait_ge(w_split, 1)
            base_step = chain[0]

            def split(c, use, h, wait):
                pool.wait_ge(w_loaded[h], use * 32 + 32)
                if wait:
                    hold(pool, multiplied, c * NB + (AHEAD - NB), pool_holds)
                high = w_parts[0:K, h, :, 0:LF]
                middle = w_parts[0:K, h, :, LF:2 * LF]
                low = w_parts[0:K, h, :, 2 * LF:3 * LF]
                raw, rest = w_raw[0:K, h], w_res[0:K, h]
                nc.gpsimd.tensor_copy(high, raw).then_inc(w_step, 1)
                pool.wait_ge(w_step, c * 4 + (base_step - 3))
                nc.gpsimd.tensor_tensor(out=rest, in0=raw, in1=high, op=ALU.subtract).then_inc(w_step, 1)
                hold(pool, w_step, c * 4 + (base_step - 2), pool_holds)
                nc.gpsimd.tensor_copy(middle, rest).then_inc(w_step, 1)
                pool.wait_ge(w_step, c * 4 + (base_step - 1))
                nc.gpsimd.tensor_tensor(out=rest, in0=rest, in1=middle, op=ALU.subtract).then_inc(w_step, 1)
                hold(pool, w_step, c * 4 + (base_step - 0), pool_holds)
                nc.gpsimd.tensor_copy(low, rest).then_inc(w_split, 1)

            split(1, 0, 1, False)
            nc.gpsimd.memset(g_w[:], 1.0).then_inc(filled, 1)
            with pool.Fori(1, CHUNKS // 2) as i:
                for h in range(2):
                    split(i * 2 + h, i, h, True)

        @block.scalar
        def _(act):
            act.dma_start(s_int[:, :, 0:N_DEC], x_dec.rearrange("(b p) n -> p b n", p=P)).then_inc(small_loaded, 16)
            act.dma_start(s_int[:, :, N_DEC:], x_cat.rearrange("(b p) n -> p b n", p=P)).then_inc(small_loaded, 16)
            act.wait_ge(s_w_clear, 1)
            act.dma_start(s_w[0:N_DEC, 0:LF], w_dec).then_inc(small_loaded, 16)
            act.dma_start(s_w[N_DEC:, LF:], w_cat).then_inc(small_loaded, 16)
            act.sem_inc(evacuated, 1)
            act.wait_ge(small_tp, 1)
            nc.scalar.copy(s_T[:, :], tp_f[0:N_SMALL, 0:NB * P]).then_inc(small_T, 1)
            for p in range(NPAIR):
                act.wait_ge(small_done, p + 1)
                nc.scalar.copy(s_sb[:, 2 * p:2 * p + 2, :],
                               acc[:, p * BANK:p * BANK + 2 * WC].rearrange("p (h n) -> p h n", h=2)[:, :, 0:2 * LF]
                               ).then_inc(saved, 1)

            def evacuate(s, h):
                act.wait_ge(transposed, s + (1 + AHEAD))
                act.wait_ge(multiplied, s + 1)
                nc.scalar.copy(xT[:, h, :], tp[:, h, 0:T * P]).then_inc(evacuated, 1)

            def save(seg, s_last, p):
                act.wait_ge(multiplied, s_last + (1 + AHEAD))
                nc.scalar.copy(sums_sb[:, seg, 2 * p:2 * p + 2, :],
                               acc[:, p * BANK:p * BANK + 2 * WC].rearrange("p (h n) -> p h n", h=2)
                               ).then_inc(saved, 1)

            for seg, (_, _, base, n, _) in enumerate(SEGS):
                with act.Fori(base * NPAIR, (base + n - 1) * NPAIR) as q:
                    for h in range(2):
                        evacuate(q * 2 + h, h)
                s0 = (base + n - 1) * NB
                for p in range(NPAIR):
                    evacuate(s0 + 2 * p, 0)
                    if p:
                        save(seg, s0 + 2 * p - 1, p - 1)
                    evacuate(s0 + 2 * p + 1, 1)
                save(seg, s0 + NB - 1, NPAIR - 1)

            act.wait_ge(maxed, STEPS)
            act.wait_ge(minus_one_ready, 1)
            nc.scalar.activation(excess[:], seen[:].rearrange("p t k -> p (t k)"), ACT.Relu, bias=minus_one[:, 0:1],
                                 accum_out=bad_f[:]).then_inc(bad_ready, 1)
            act.wait_ge(general_ready, 1)
            with act.If(act.value_load(general[0:1, 0:1], min_val=0, max_val=1) > 0):
                k0 = 0
                for s, (x, w, _, n, col) in enumerate(SEGS):
                    with act.Fori(0, NB) as b:
                        with act.Fori(0, n) as c:
                            act.wait_ge(g_tp, b * n + c + (k0 + 1))
                            nc.scalar.copy(g_T[:, :], tp_f[0:K, 0:T * P]).then_inc(g_xT, 1)
                        act.wait_ge(g_mult, b * n + (k0 + n + 1))
                        act.wait_ge(g_fin, b + (s * NB + 1))
                        nc.scalar.copy(g_sb[:, :], acc[:, 0:LF + 1]).then_inc(g_saved, 1)
                    k0 += NB * n

        @block.vector
        def _(dve):
            chain = [0]

            def link(ins):
                chain[0] += 1
                ins.then_inc(dve_step, 1)
                dve.wait_ge(dve_step, chain[0])

            def across(r, n):
                return r.unsqueeze(2).to_broadcast([P, n, LF])

            def nonzero(s, counts):
                return nc.vector.scalar_tensor_tensor(out=s, in0=counts, scalar=0.0, in1=counts,
                                                      op0=ALU.is_equal, op1=ALU.add)

            def small_finish():
                dve.wait_ge(saved, NPAIR)
                for slot, (a, z) in enumerate(((0, N_DEC), (N_DEC, N_SMALL))):
                    n, s, r = count[:, slot, :], safe[:, slot, :], recip[:, slot, :]
                    link(nc.vector.tensor_reduce(n, s_f[:, :, a:z], AX.X, ALU.add))
                    link(nonzero(s, n))
                    link(nc.vector.reciprocal(r, s))
                    dst = dec_once[:, :, :] if slot == 0 else out_sb[:, :, 2 * LF:3 * LF]
                    link(nc.vector.tensor_tensor(dst, s_sb[:, :, slot * LF:(slot + 1) * LF], across(r, NB), ALU.mult))

            def finish(seg, lo, hi):
                sums = sums_sb[:, seg, lo:hi, :]
                n = hi - lo
                col = SEGS[seg][4]
                dst = out_sb[:, lo:hi, col:col + LF]
                dve.wait_ge(saved, NPAIR * (seg + 1) + hi // 2)
                s, r, lower = safe[:, 2, lo:hi], recip[:, 2, lo:hi], half[:, lo:hi]
                full = dst if seg == 0 else whole[:, lo:hi]
                at = chain[0]
                chain[0] += 4
                nonzero(s, sums[:, :, 3 * LF]).then_inc(dve_step, 1)
                nc.vector.tensor_tensor(lower, sums[:, :, LF:2 * LF], sums[:, :, 2 * LF:3 * LF], ALU.add
                                        ).then_inc(dve_step, 1)
                dve.wait_ge(dve_step, at + 1)
                nc.vector.reciprocal(r, s).then_inc(dve_step, 1)
                dve.wait_ge(dve_step, at + 2)
                nc.vector.tensor_tensor(full, lower, sums[:, :, 0:LF], ALU.add).then_inc(dve_step, 1)
                dve.wait_ge(dve_step, at + 4)
                if seg == 0:
                    nc.vector.tensor_tensor(out_sb[:, lo:hi, 0:LF], dec_once[:, lo:hi], across(r, n),
                                            ALU.mult).then_inc(finished, 1)
                else:
                    nc.vector.tensor_tensor(dst, full, across(r, n), ALU.mult).then_inc(finished, 1)

            def round_step(c, b):
                dve.wait_ge(x_loaded[b], c * 16 + 16)
                dve.wait_ge(transposed, c * NB + (b + 1))
                nc.vector.tensor_copy(x_bf[:, b % 2, :, 0:K],
                                      x_int[:, b, :].bitcast(u32).rearrange("p (k t) -> p t k", t=T)
                                      ).then_inc(cast, 1)

            def max_step(c, b):
                dve.wait_ge(cast, c * NB + (b + 1))
                if not (isinstance(c, int) and c == 0 and b == 0):
                    dve.wait_ge(maxed, c * NB + b)
                nc.vector.tensor_tensor(seen[:, :, :], seen[:, :, :], x_bf[:, b % 2, :, :], ALU.max).then_inc(maxed, 1)

            def round_steps(c, tiles):
                for b in tiles:
                    round_step(c, b)
                    max_step(c, b)

            nc.vector.memset(s_w[:], 0.0).then_inc(s_w_clear, 1)
            nc.vector.memset(zeros[:].bitcast(u32), 0).then_inc(zeroed, 1)
            nc.vector.memset(minus_one[:], -1.0).then_inc(minus_one_ready, 1)
            link(nc.vector.memset(x_bf[:, :, :, K:].rearrange("p h t k -> p (h t) k"), 0.0))
            link(nc.vector.memset(w_parts[96:, :, :, 0:3 * LF], 0.0))
            link(nc.vector.memset(seen[:].bitcast(u32), 0))

            dve.wait_ge(w_loaded[0], 32)
            rest, raw = w_res[0:K, 0], w_raw[0:K, 0]
            high, middle, low = (w_parts[0:K, 0, :, n * LF:(n + 1) * LF] for n in range(3))
            link(nc.vector.tensor_copy(high, raw))
            link(nc.vector.tensor_tensor(rest, raw, high, ALU.subtract))
            link(nc.vector.tensor_copy(middle, rest))
            link(nc.vector.tensor_tensor(rest, rest, middle, ALU.subtract))
            nc.vector.tensor_copy(low, rest).then_inc(w_split, 1)

            dve.wait_ge(small_loaded, 64)
            nc.vector.tensor_copy(s_f[:, :, :], s_int[:, :, :]).then_inc(small_cast, 1)
            for seg, (_, _, base, n, _) in enumerate(SEGS):
                round_steps(base, range(NB))
                if seg == 0:
                    small_finish()
                else:
                    finish(seg - 1, 0, NB)
                if seg < LAST:
                    with dve.Fori(base + 1, base + n) as c:
                        round_steps(c, range(NB))
            for c in range(SEGS[LAST][2] + 1, CHUNKS - 1):
                round_steps(c, range(NB))
            round_steps(CHUNKS - 1, range(NB - 2))
            dve.wait_ge(maxed, STEPS - 2)
            for b in (NB - 2, NB - 1):
                round_step(CHUNKS - 1, b)
            finish(LAST, 0, 2)
            for b in (NB - 2, NB - 1):
                max_step(CHUNKS - 1, b)
            for p in range(1, NPAIR):
                finish(LAST, 2 * p, 2 * p + 2)
            dve.wait_ge(bad_summed, 1)
            nc.vector.tensor_scalar(general[:], tp_f[0:1, 0:1], 0.0, None, ALU.is_gt).then_inc(general_ready, 1)
            dve.wait_ge(general_ready, 1)
            with dve.If(dve.value_load(general[0:1, 0:1], min_val=0, max_val=1) > 0):
                k0 = stored_before = steps_before = 0
                for s, (x, w, _, n, col) in enumerate(SEGS):
                    with dve.Fori(0, NB) as b:
                        with dve.Fori(0, n) as c:
                            dve.wait_ge(g_x_loaded, (b * n + c + (k0 + 1)) * 16)
                            nc.vector.tensor_copy(g_f[:, :, :], g_int[:, :].rearrange("p (k t) -> p t k", t=T)
                                                  ).then_inc(g_cast, 1)
                        dve.wait_ge(g_saved, b + (s * NB + 2))
                        dve.wait_ge(g_stored, b * (16 * G_STORES[s]) + (16 + stored_before))
                        steps = b * G_STEPS[s] + steps_before
                        total = g_sb[:, LF:LF + 1]
                        nc.vector.tensor_scalar(g_zero[:], total, 0.0, None, ALU.is_equal).then_inc(g_step, 1)
                        dve.wait_ge(g_step, steps + 1)
                        nc.vector.tensor_tensor(g_safe[:], g_zero[:], total, ALU.add).then_inc(g_step, 1)
                        dve.wait_ge(g_step, steps + 2)
                        nc.vector.reciprocal(g_recip[:], g_safe[:]).then_inc(g_step, 1)
                        dve.wait_ge(g_step, steps + 3)
                        if s == 0:
                            nc.vector.tensor_copy(g_out[:], g_sb[:, 0:LF]).then_inc(g_step, 1)
                            dve.wait_ge(g_step, steps + 4)
                            nc.vector.tensor_scalar(g_dec[:], dec_once[:, bass.ds(b, 1), :].rearrange("p a f -> p (a f)"),
                                                    g_recip[:], None, ALU.mult).then_inc(g_fin, 1)
                        else:
                            nc.vector.tensor_scalar(g_out[:], g_sb[:, 0:LF], g_recip[:], None,
                                                    ALU.mult).then_inc(g_fin, 1)
                    stored_before += 16 * G_STORES[s] * NB
                    steps_before += G_STEPS[s] * NB
                    k0 += NB * n

        @block.tensor
        def _(pe):
            pe.wait_ge(ident_ready, 2)
            pe.wait_ge(small_cast, 1)
            for b in range(NB):
                last = nc.tensor.transpose(tp_f[0:N_SMALL, b * P:(b + 1) * P], s_f[:, b, :], ident_f[:, :])
            last.then_inc(small_tp, 1)
            pe.wait_ge(small_T, 1)
            pe.wait_ge(small_loaded, 64)
            for b in range(NB):
                last = nc.tensor.matmul(acc_at(b // 2, b % 2, 2 * LF), s_T[:, b * P:(b + 1) * P], s_w[:, :],
                                        start=True, stop=True)
                if b % 2:
                    last.then_inc(small_done, 1)
            pe.sem_inc(transposed, AHEAD)
            pe.sem_inc(multiplied, AHEAD)

            def transpose_step(s, h):
                pe.wait_ge(cast, s + 1)
                if not isinstance(s, int) or s >= 2:
                    pe.wait_ge(evacuated, s)
                for t in range(T):
                    last = nc.tensor.transpose(tp[:, h, t * P:(t + 1) * P], x_bf[:, h, t, :], ident[:, :])
                last.then_inc(transposed, 1)

            def multiply_step(s, h, wh, pair):
                pe.wait_ge(evacuated, s + 2)
                for t in range(T):
                    last = nc.tensor.matmul(acc_at(pair, h, WC), xT[:, h, t * P:(t + 1) * P], w_parts[:, wh, t, :],
                                            start=False, stop=(t == T - 1), skip_group_check=True)
                last.then_inc(multiplied, 1)

            transpose_step(0, 0)
            pe.wait_ge(filled, 2)
            pe.wait_ge(zeroed, 1)
            for seg, (_, _, base, n, _) in enumerate(SEGS):
                for p in range(NPAIR):
                    pe.wait_ge(saved, seg * NPAIR + p + 1)
                    nc.tensor.matmul(acc[:, p * BANK:(p + 1) * BANK], zeros[:, 0:P], zeros[:, :],
                                     start=True, stop=True)
                final = seg == len(SEGS) - 1
                with ExitStack() as pairs:
                    i = pairs.enter_context(pe.Fori(0, n // 2)) if n > 2 else 0
                    for wh in range(2):
                        c = i * 2 + (base + wh)
                        hold(pe, w_split, c + 1, pe_holds)
                        rolled = NPAIR - 1 if final and wh == 1 else NPAIR
                        with pe.Fori(0, rolled) as pair:
                            for h in range(2):
                                s = c * NB + pair * 2 + h
                                transpose_step(s + 1, 1 - h)
                                multiply_step(s, h, wh, pair)
                        if rolled < NPAIR:
                            transpose_step(STEPS - 1, 1)
                            multiply_step(STEPS - 2, 0, wh, NPAIR - 1)
                            multiply_step(STEPS - 1, 1, wh, NPAIR - 1)

            pe.wait_ge(bad_ready, 1)
            nc.tensor.matmul(tp_f[0:1, 0:1], bad_f[:, :], ones_col[:, :], start=True, stop=True).then_inc(bad_summed, 1)
            pe.wait_ge(general_ready, 1)
            with pe.If(pe.value_load(general[0:1, 0:1], min_val=0, max_val=1) > 0):
                pe.wait_ge(filled, 3)
                pe.sem_inc(g_mult, 1)
                pe.sem_inc(g_stored, 16)
                pe.sem_inc(g_fin, 1)
                pe.sem_inc(g_saved, 1)
                pe.wait_ge(saved, (len(SEGS) + 1) * NPAIR)
                k0 = 0
                for s, (x, w, _, n, col) in enumerate(SEGS):
                    with pe.Fori(0, NB) as b:
                        pe.wait_ge(g_saved, b + (s * NB + 1))
                        nc.tensor.matmul(acc[:, 0:LF + 1], zeros[:, 0:P], zeros[:, 0:LF + 1], start=True, stop=True)
                        with pe.Fori(0, n) as c:
                            k = b * n + c + k0
                            pe.wait_ge(g_cast, k + 1)
                            for t in range(T):
                                last = nc.tensor.transpose(tp_f[0:K, t * P:(t + 1) * P], g_f[:, t, :], ident_f[:, :])
                            last.then_inc(g_tp, 1)
                            pe.wait_ge(g_xT, k + 1)
                            pe.wait_ge(g_w_loaded, (k + 1) * 32)
                            for t in range(T):
                                last = nc.tensor.matmul(acc[:, 0:LF + 1], g_T[:, t * P:(t + 1) * P], g_w[:, t, :],
                                                        start=False, stop=(t == T - 1), skip_group_check=True)
                            last.then_inc(g_mult, 1)
                    k0 += NB * n


_INS = ['r_decade_idxs', 'r_movie_idxs', 'r_category_idxs', 'r_person_idxs', 'r_company_idxs',
        'L0_rec_W_dec', 'L0_rec_W_mov', 'L0_rec_W_cat', 'L0_rec_W_per', 'L0_rec_W_com']


def kernel(**inputs):
    import numpy as _np
    import concourse.bacc as _bacc
    from concourse import mybir as _mybir
    from concourse.bass_utils import run_bass_kernel_spmd as _run

    nc = _bacc.Bacc("TRN2", target_bir_lowering=False, num_devices=1)
    arrays, args = {}, []
    for name in _INS:
        a = _np.ascontiguousarray(inputs[name])
        arrays[f"in_{name}_dram"] = a
        args.append(nc.dram_tensor(f"in_{name}_dram", a.shape, _mybir.dt.from_np(a.dtype), kind="ExternalInput").ap())
    rows = inputs['r_movie_idxs'].shape[0]
    cols = 5 * inputs['L0_rec_W_mov'].shape[1]
    out = nc.dram_tensor("out_0_dram", (rows, cols), _mybir.dt.float32, kind="ExternalOutput").ap()
    recommender_program(nc, *args, out)
    r = _run(nc, [arrays], core_ids=[0])
    return r.results[0]["out_0_dram"]
```
